# Optimizing a Trainium2 kernel written in Bass

```python
import numpy as np
import jax
import jax.numpy as jnp

def _softmax(x, axis=-1):
    return jax.nn.softmax(x, axis=axis)
def _gelu(x):
    return jax.nn.gelu(x, approximate=True)
def _silu(x):
    return jax.nn.silu(x)
def _sigmoid(x):
    return jax.nn.sigmoid(x)
def _layernorm(x, axis=-1, eps=1e-5):
    m = jnp.mean(x, axis=axis, keepdims=True)
    v = jnp.var(x, axis=axis, keepdims=True)
    return (x - m) / jnp.sqrt(v + eps)
def _scatter_add(tgt, idx, src, axis=0):
    return tgt.at[idx].add(src)
def _segment_sum(src, seg, n):
    return jax.ops.segment_sum(src, seg, n)

kernel_name = 'mk_adj_seq_d2_adj_256_106f50'

def setup_inputs(seed: int = 0):
    np.random.seed(seed)
    _w = jnp.asarray
    def _rec_inputs():
        import jax
        import jax.numpy as jnp
        _gk = jax.random.key(seed)
        x = -0.0005207 + 1.001 * jax.random.normal(jax.random.fold_in(_gk, 1), (64, 256, 256), jnp.float32)
        _a = jax.random.bernoulli(jax.random.fold_in(_gk, 2), 0.03125, (64, 256, 256))
        _a = jnp.logical_or(_a, jnp.swapaxes(_a, -1, -2))
        _a = jnp.logical_or(_a, jnp.eye(256, dtype=bool))
        adj = _a.astype(jnp.int32)
        return x, adj
    x, adj = _rec_inputs()
    def _L0_gnn_setup():
        import jax, jax.numpy as jnp
        import numpy as np
        B, N, D = (8, 1024, 256)
        H = 8
        DH = D // H
        R = 4
        FF = 1024
        EPS = 1e-05

        def _lin(k, fan_in, shape):
            return jax.random.normal(k, shape, jnp.float32) * (1.0 / np.sqrt(fan_in))

        def _ln(x, g, b):
            m = x.mean(-1, keepdims=True)
            v = ((x - m) ** 2).mean(-1, keepdims=True)
            return (x - m) * jax.lax.rsqrt(v + EPS) * g + b
        key = jax.random.key(seed)
        ks = jax.random.split(key, 16)
        src = jax.random.normal(ks[0], (B, N, D), jnp.float32)
        adj_matrix = jax.random.randint(ks[1], (B, N, N), 0, 5, dtype=jnp.int32)
        Wq = _lin(ks[2], D, (D, D))
        bq = jnp.zeros((D,), jnp.float32)
        Wk = _lin(ks[3], D, (D, D))
        bk = jnp.zeros((D,), jnp.float32)
        Wv = _lin(ks[4], D, (R, D, D))
        bv = jnp.zeros((R, D), jnp.float32)
        Wo = _lin(ks[5], D, (D, D))
        bo = jnp.zeros((D,), jnp.float32)
        W1 = _lin(ks[6], D, (D, FF))
        b1 = jnp.zeros((FF,), jnp.float32)
        W2 = _lin(ks[7], FF, (FF, D))
        b2 = jnp.zeros((D,), jnp.float32)
        g1 = jnp.ones((D,), jnp.float32)
        beta1 = jnp.zeros((D,), jnp.float32)
        g2 = jnp.ones((D,), jnp.float32)
        beta2 = jnp.zeros((D,), jnp.float32)
        return dict(src=src, adj_matrix=adj_matrix, Wq=Wq, bq=bq, Wk=Wk, bk=bk, Wv=Wv, bv=bv, Wo=Wo, bo=bo, W1=W1, b1=b1, W2=W2, b2=b2, g1=g1, beta1=beta1, g2=g2, beta2=beta2)
    _L0_gnn_all = _L0_gnn_setup()
    _L0_gnn_in = {k: v for k, v in _L0_gnn_all.items() if k in ('Wq', 'bq', 'Wk', 'bk', 'Wv', 'bv', 'Wo', 'bo', 'W1', 'b1', 'W2', 'b2', 'g1', 'beta1', 'g2', 'beta2', )}
    del _L0_gnn_all

    def _L1_gnn_setup():
        import jax, jax.numpy as jnp
        import numpy as np
        ALPHA = 0.2
        EPS = 1e-05
        NEG = -9000000000000000.0
        H, DH = (8, 32)

        def _layernorm(x, g, b):
            mu = jnp.mean(x, axis=-1, keepdims=True)
            var = jnp.mean(jnp.square(x - mu), axis=-1, keepdims=True)
            return (x - mu) * jax.lax.rsqrt(var + EPS) * g + b
        key = jax.random.key(seed)
        ks = jax.random.split(key, 6)
        w, n, d = (4, 2048, 256)
        feats = jax.random.normal(ks[0], (w, n, d), dtype=jnp.float32)
        adj = jax.random.randint(ks[1], (w, n, n), 0, 2, dtype=jnp.int32)
        adj = adj.at[:, jnp.arange(n), jnp.arange(n)].set(1)
        s = 0.06
        Wq = jax.random.normal(ks[2], (d, H * DH), dtype=jnp.float32) * s
        Wk = jax.random.normal(ks[3], (d, H * DH), dtype=jnp.float32) * s
        Wv = jax.random.normal(ks[4], (d, H * DH), dtype=jnp.float32) * s
        Wffn = jax.random.normal(ks[5], (H * DH, H * DH + d), dtype=jnp.float32) * 0.05
        g1 = jnp.ones((H * DH,), jnp.float32)
        b1 = jnp.zeros((H * DH,), jnp.float32)
        g2 = jnp.ones((H * DH,), jnp.float32)
        b2 = jnp.zeros((H * DH,), jnp.float32)
        return {'features': feats, 'adj': adj, 'Wq': Wq, 'Wk': Wk, 'Wv': Wv, 'Wffn': Wffn, 'g1': g1, 'b1': b1, 'g2': g2, 'b2': b2}
    _L1_gnn_all = _L1_gnn_setup()
    _L1_gnn_in = {k: v for k, v in _L1_gnn_all.items() if k in ('Wq', 'Wk', 'Wv', 'Wffn', 'g1', 'b1', 'g2', 'b2', )}
    del _L1_gnn_all

    return {
        "x": x,
        "adj": adj,
        "L0_gnn_Wq": _L0_gnn_in["Wq"],
        "L0_gnn_bq": _L0_gnn_in["bq"],
        "L0_gnn_Wk": _L0_gnn_in["Wk"],
        "L0_gnn_bk": _L0_gnn_in["bk"],
        "L0_gnn_Wv": _L0_gnn_in["Wv"],
        "L0_gnn_bv": _L0_gnn_in["bv"],
        "L0_gnn_Wo": _L0_gnn_in["Wo"],
        "L0_gnn_bo": _L0_gnn_in["bo"],
        "L0_gnn_W1": _L0_gnn_in["W1"],
        "L0_gnn_b1": _L0_gnn_in["b1"],
        "L0_gnn_W2": _L0_gnn_in["W2"],
        "L0_gnn_b2": _L0_gnn_in["b2"],
        "L0_gnn_g1": _L0_gnn_in["g1"],
        "L0_gnn_beta1": _L0_gnn_in["beta1"],
        "L0_gnn_g2": _L0_gnn_in["g2"],
        "L0_gnn_beta2": _L0_gnn_in["beta2"],
        "L1_gnn_Wq": _L1_gnn_in["Wq"],
        "L1_gnn_Wk": _L1_gnn_in["Wk"],
        "L1_gnn_Wv": _L1_gnn_in["Wv"],
        "L1_gnn_Wffn": _L1_gnn_in["Wffn"],
        "L1_gnn_g1": _L1_gnn_in["g1"],
        "L1_gnn_b1": _L1_gnn_in["b1"],
        "L1_gnn_g2": _L1_gnn_in["g2"],
        "L1_gnn_b2": _L1_gnn_in["b2"],
    }

def reference(x, adj, L0_gnn_Wq, L0_gnn_bq, L0_gnn_Wk, L0_gnn_bk, L0_gnn_Wv, L0_gnn_bv, L0_gnn_Wo, L0_gnn_bo, L0_gnn_W1, L0_gnn_b1, L0_gnn_W2, L0_gnn_b2, L0_gnn_g1, L0_gnn_beta1, L0_gnn_g2, L0_gnn_beta2, L1_gnn_Wq, L1_gnn_Wk, L1_gnn_Wv, L1_gnn_Wffn, L1_gnn_g1, L1_gnn_b1, L1_gnn_g2, L1_gnn_b2):
    import jax
    import jax.numpy as jnp
    def _L0_gnn_ref(src, adj_matrix, Wq, bq, Wk, bk, Wv, bv, Wo, bo, W1, b1, W2, b2, g1, beta1, g2, beta2):
        import jax, jax.numpy as jnp
        import numpy as np
        B, N, D = (8, 1024, 256)
        H = 8
        DH = D // H
        R = 4
        FF = 1024
        EPS = 1e-05

        def _lin(k, fan_in, shape):
            return jax.random.normal(k, shape, jnp.float32) * (1.0 / np.sqrt(fan_in))

        def _ln(x, g, b):
            m = x.mean(-1, keepdims=True)
            v = ((x - m) ** 2).mean(-1, keepdims=True)
            return (x - m) * jax.lax.rsqrt(v + EPS) * g + b
        Bb, Nn, Dm = src.shape
        h, dh = (H, Dm // H)
        q = (src @ Wq + bq).reshape(Bb, Nn, h, dh).transpose(0, 2, 1, 3)
        k = (src @ Wk + bk).reshape(Bb, Nn, h, dh).transpose(0, 2, 1, 3)
        scores = jnp.einsum('bhid,bhjd->bhij', q, k) / np.sqrt(dh)
        attn = jax.nn.softmax(scores, axis=-1)
        out = jnp.zeros_like(q)
        for r in range(Wv.shape[0]):
            v_r = (src @ Wv[r] + bv[r]).reshape(Bb, Nn, h, dh).transpose(0, 2, 1, 3)
            mask = (adj_matrix == r)[:, None]
            out = out + jnp.einsum('bhij,bhjd->bhid', attn * mask, v_r)
        attn_out = out.transpose(0, 2, 1, 3).reshape(Bb, Nn, Dm) @ Wo + bo
        x = _ln(src + attn_out, g1, beta1)
        ff = jax.nn.gelu(x @ W1 + b1, approximate=False) @ W2 + b2
        return _ln(x + ff, g2, beta2)

    def _L1_gnn_ref(features, adj, Wq, Wk, Wv, Wffn, g1, b1, g2, b2):
        import jax, jax.numpy as jnp
        import numpy as np
        ALPHA = 0.2
        EPS = 1e-05
        NEG = -9000000000000000.0
        H, DH = (8, 32)

        def _layernorm(x, g, b):
            mu = jnp.mean(x, axis=-1, keepdims=True)
            var = jnp.mean(jnp.square(x - mu), axis=-1, keepdims=True)
            return (x - mu) * jax.lax.rsqrt(var + EPS) * g + b
        w, n, d = features.shape

        def heads(x):
            return x.reshape(w, n, H, DH).transpose(0, 2, 1, 3)
        q = heads(features @ Wq)
        k = heads(features @ Wk)
        v = heads(features @ Wv)
        e = jnp.einsum('whqd,whkd->whqk', q, k)
        e = jnp.where(e >= 0, e, ALPHA * e)
        attn = jax.nn.softmax(jnp.where(adj[:, None] > 0, e, NEG), axis=-1)
        h = jnp.einsum('whqk,whkd->whqd', attn, v)
        h = h.transpose(0, 2, 1, 3).reshape(w, n, H * DH)
        out = _layernorm(h, g1, b1)
        out = jnp.concatenate([out, features], axis=-1) @ Wffn.T
        out = _layernorm(out, g2, b2)
        return out + features

    x = _L0_gnn_ref(x, adj, L0_gnn_Wq, L0_gnn_bq, L0_gnn_Wk, L0_gnn_bk, L0_gnn_Wv, L0_gnn_bv, L0_gnn_Wo, L0_gnn_bo, L0_gnn_W1, L0_gnn_b1, L0_gnn_W2, L0_gnn_b2, L0_gnn_g1, L0_gnn_beta1, L0_gnn_g2, L0_gnn_beta2)
    x = _L1_gnn_ref(x, adj, L1_gnn_Wq, L1_gnn_Wk, L1_gnn_Wv, L1_gnn_Wffn, L1_gnn_g1, L1_gnn_b1, L1_gnn_g2, L1_gnn_b2)
    return x


_drawn_inputs = setup_inputs


def setup_inputs(seed=0):
    import zlib

    import numpy as np

    out = dict(_drawn_inputs(seed))
    spreads = {'L0_gnn_bq': (0.0, 0.453),
     'L0_gnn_bk': (0.0, 0.8),
     'L0_gnn_bv': (0.0, 0.1),
     'L0_gnn_bo': (0.0, 0.1),
     'L0_gnn_b1': (0.0, 0.1),
     'L0_gnn_b2': (0.0, 0.1),
     'L0_gnn_g1': (1.0, 0.2),
     'L0_gnn_beta1': (0.0, 0.1),
     'L0_gnn_g2': (1.0, 0.2),
     'L0_gnn_beta2': (0.0, 0.1),
     'L1_gnn_g1': (1.0, 0.2),
     'L1_gnn_b1': (0.0, 0.1),
     'L1_gnn_g2': (1.0, 0.2),
     'L1_gnn_b2': (0.0, 0.1)}
    factors = {}
    for name, (base, spread) in spreads.items():
        noise = np.random.default_rng([zlib.crc32(name.encode()), seed]).standard_normal(out[name].shape)
        drawn = base * np.exp(spread * noise) if base else spread * noise
        out[name] = jnp.asarray(drawn.astype(out[name].dtype))
    for name, factor in factors.items():
        out[name] = (out[name] * factor).astype(out[name].dtype)
    return out
```

```python
import concourse.bass as bass
from concourse import mybir
from contextlib import ExitStack

G, N, D = 64, 256, 256
H = 8
DH = D // H
FF = 1024
P = 128
NT = N // P
KT = D // P
FT = FF // P
GH = P // DH
NG = H // GH
PAIRS = H // 2
CH = 2
NCH = FT // CH
STK = 3 * DH
SHIFT = 64
EPS = 1e-5
NEG = -9e15
ALPHA = 0.2
SCALE = float(DH) ** -0.5
TERMS = 3
BANKS = 4

F32 = mybir.dt.float32
F32R = mybir.dt.float32r
BF16 = mybir.dt.bfloat16
I32 = mybir.dt.int32
ALU = mybir.AluOpType
ACT = mybir.ActivationFunctionType
AX = mybir.AxisListType


class Signal:

    def __init__(self, sem, per):
        self.sem, self.per = sem, per

    def at(self, graph, n=None):
        return graph * self.per + (self.per if n is None else n)

    def before(self, graph):
        return (graph - 1) * self.per + self.per


def later(graph):
    return graph is not None and not (isinstance(graph, int) and graph == 0)


def turns(eng, body):
    body(None, None, 0)
    body(None, 0, 1)
    body(0, 1, 2)
    with eng.Fori(1, G - 2) as i:
        body(i, i + 1, i + 2)
    body(G - 2, G - 1, None)
    body(G - 1, None, None)


class Path:
    general = False


def build(nc, x, xT, adj, adjT, w):
    ctx = ExitStack()
    with ctx:
        out = w["out"]

        def sb(name, shape, dt=F32):
            return ctx.enter_context(nc.sbuf_tensor(name, shape, dt))

        def hilo(name, shape):
            return sb(name + "_hi", shape, F32R), sb(name + "_lo", shape, F32R)

        def sem(name):
            return ctx.enter_context(nc.semaphore(name))

        def sig(name, per=1):
            return Signal(sem(name), per)

        WNAMES = [("wq", KT, D), ("wk", KT, D), ("wo", KT, D), ("w1", KT, FF), ("w2", FT, D),
                  ("lq", KT, D), ("lk", KT, D), ("lv", KT, D), ("wf", 2 * KT, D)]
        W = {n: hilo(n, [P, t, c]) for n, t, c in WNAMES}
        W["wv"] = hilo("wv", [P, KT, 2 * D])
        bias_col = sb("bias_col", [P, 2 * KT + FT])
        bq_c, bk_c, b1_c = (bias_col[:, 0:KT], bias_col[:, KT:2 * KT], bias_col[:, 2 * KT:])
        bias_r = sb("bias_r", [SHIFT, 4 * D], F32R)
        bv_r, bo_r, b2_r = bias_r[:, 0:2 * D], bias_r[:, 2 * D:3 * D], bias_r[:, 3 * D:]
        norm = sb("norm", [P, 8, D])
        G1, E1, G2, E2, LG1, LB1, LG2, LB2 = range(8)

        ident = sb("ident", [P, P])
        identb = sb("identb", [P, P], BF16)
        ones = sb("ones", [P, P])
        onesr = sb("onesr", [SHIFT, P], F32R)
        selr = sb("selr", [SHIFT, H], F32R)
        power = sb("power", [P, NT])
        eps = sb("eps", [P, NT])
        known = sb("known", [P, 1])
        lowest = sb("lowest", [P, 1])
        bad = sb("bad", [P, 1])
        flag = sb("flag", [1, 1], I32)
        carrier = sb("carrier", [P, 2])

        xt = sb("xt", [P, KT, N])
        xn = sb("xn", [P, NT, D])
        adj_a = sb("adj_a", [P, NT, N], I32)
        adj_q = sb("adj_q", [P, NT, N], I32)
        adj_k = sb("adj_k", [P, NT, N], I32)
        rel1 = sb("rel1", [P, NT, N], BF16)
        off_q = sb("off_q", [P, NT, N], BF16)
        off_k = sb("off_k", [P, NT, N], BF16)
        xt_hi, xt_lo = hilo("xt_r", [P, KT, N])
        qk_hi, qk_lo = hilo("qk", [P, 2, NG, N])
        stack_a = sb("stack_a", [STK, 2, H, N], F32R)
        stack_r = sb("stack_r", [STK, 2, H, N], F32R)
        v_a = sb("v_a", [P, NT, 2, D])
        v_r = sb("v_r", [P, NT, D])
        mx_a = sb("mx_a", [P, NT, H])
        mx_r = sb("mx_r", [P, NT, H])
        low_max = sb("low_max", [H, N])
        leaky = sb("leaky", [H, N])
        shift_a = sb("shift_a", [SHIFT, N], F32R)
        shift_r = sb("shift_r", [SHIFT, N], F32R)
        probs = sb("probs", [P, NG, GH, NT, N])
        probs1 = sb("probs1", [P, GH, NT, N])
        att = sb("att", [P, NG, N])
        att_hi, att_lo = hilo("att_r", [P, NG, N])
        res = sb("res", [P, NT, D])
        x1 = sb("x1", [P, NT, D])
        x1t_hi, x1t_lo = xt_hi, xt_lo
        act = sb("act", [P, 2, CH, N])
        act_hi, act_lo = hilo("act_r", [P, 2, CH, N])
        x2 = sb("x2", [P, NT, D])
        x2t_hi, x2t_lo = hilo("x2t", [P, KT, N])
        n1 = sb("n1", [P, NT, D])
        n1t_hi, n1t_lo = att_hi, att_lo
        y = n1
        result = res
        stats = sb("stats", [P, 4, NT, 6])
        mv = sb("mv", [P, 4, NT, 2])
        rstd = sb("rstd", [P, 4, 2, NT])

        scores = [ctx.enter_context(nc.psum_tensor(f"scores{s}", [P, 2, NT, N], F32)) for s in range(2)]
        bank = [ctx.enter_context(nc.psum_tensor(f"bank{b}", [P, 2, N], F32)) for b in range(BANKS)]
        B_X1T, B_UP, B_DOWN, B_X2T = 0, (1, 2, 0, 1), 3, 2
        B_RQ, B_RK, B_RV = 0, 1, 2
        B_AMT, B_AO, B_ADEN, B_WO = 0, 1, 3, 2
        B_RMT, B_RO, B_RDEN = 0, 1, 3
        B_Q, B_K, B_V = 0, 1, (3, 0)
        B_HN, B_N1T, B_FFN = 2, 1, 2

        ld_xt, ld_xn, ld_adj_a = sig("ld_xt", 16), sig("ld_xn", 16), sig("ld_adj_a", 16)
        ld_adj_r = sig("ld_adj_r", 32)
        xt_hi_done, xt_split = sig("xt_hi_done"), sig("xt_split")
        rel1_done, off_done = sig("rel1_done"), sig("off_done", 2)
        q_mm, v_mm = sig("q_mm", 2), sig("v_mm", 2)
        qk_hi_done, qk_split, v_done = sig("qk_hi_done", 2), sig("qk_split", 2), sig("v_done", 2)
        stacked_a = [sig(f"stacked_a{h}", 16 * 6) for h in range(GH)]
        sa_mm, mx_a_done, amt_mm = sig("sa_mm", PAIRS), sig("mx_a_done", PAIRS), sig("amt_mm")
        ashift_hi, ashift = sig("ashift_hi"), sig("ashift")
        sta_mm, probs_a, probs1_done = sig("sta_mm", PAIRS), sig("probs_a", PAIRS), sig("probs1_done", PAIRS)
        pva_mm, pv1_mm = sig("pva_mm", NG), sig("pv1_mm", NG)
        rden_a, att_a, att_hi_done, att_split = sig("rden_a"), sig("att_a"), sig("att_hi_done"), sig("att_split")
        wo_mm, res_a_done = sig("wo_mm"), sig("res_a_done")
        ln = ["ln_a", "ln_m", "ln_h", "ln_o"]
        LN_A, LN_M, LN_H, LN_O = range(4)
        ln_stats = [sig(n + "_stats", 2) for n in ln]
        ln_mv = [sig(n + "_mv", 2) for n in ln]
        ln_var = [sig(n + "_var") for n in ln]
        ln_rstd = [sig(n + "_rstd") for n in ln]
        ln_mid = [sig(n + "_mid", 2) for n in ln]
        ln_done = [sig(n + "_done", 2) for n in ln]
        x1t_mm, x1t_hi_done, x1t_split = sig("x1t_mm"), sig("x1t_hi_done"), sig("x1t_split")
        up_mm, act_done, act_hi_done, act_split = (sig("up_mm", NCH), sig("act_done", NCH),
                                                   sig("act_hi_done", NCH), sig("act_split", NCH))
        down_mm, down_part, res_m_done = sig("down_mm"), sig("down_part", NCH), sig("res_m_done")
        x2t_mm, x2t_hi_done, x2t_split = sig("x2t_mm"), sig("x2t_hi_done"), sig("x2t_split")
        rq_mm, rv_mm = sig("rq_mm", 2), sig("rv_mm")
        rqk_hi_done, rqk_split, rv_done = sig("rqk_hi_done", 2), sig("rqk_split", 2), sig("rv_done")
        stacked_r = [sig(f"stacked_r{h}", 16 * 6) for h in range(GH)]
        sr_mm, mx_r_done, rmt_mm = sig("sr_mm", PAIRS), sig("mx_r_done", PAIRS), sig("rmt_mm")
        low_max_done = sig("low_max_done")
        leaky_done, rshift_hi, rshift = sig("leaky_done"), sig("rshift_hi"), sig("rshift")
        str_mm, low_done, leaky_scores, sub_mm, probs_r = (sig("str_mm", PAIRS), sig("low_done", PAIRS), sig("leaky_scores", PAIRS),
                                               sig("sub_mm", PAIRS), sig("probs_r", PAIRS))
        pvr_mm, rden_r, att_r_done = sig("pvr_mm", NG), sig("rden_r"), sig("att_r_done")
        hn_mm, n1t_mm, n1t_hi_done, n1t_split = sig("hn_mm"), sig("n1t_mm"), sig("n1t_hi_done"), sig("n1t_split")
        ffn_mm, result_done, stored = sig("ffn_mm"), sig("result_done"), sig("stored", 16)
        known_done, lowest_done = sig("known_done"), sig("lowest_done")
        bad_done, bad_mm, flag_ready = sem("bad_done"), sem("bad_mm"), sem("flag_ready")
        x_loaded, x_diff, x_high, x_ready = sig("x_loaded", 128), sig("x_diff", 4), sig("x_high", 4), sig("x_ready", 4)
        x_v, x_vr = sig("x_v", 2), sig("x_vr", TERMS)
        x_masked, x_mask_part = sig("x_masked", TERMS), sig("x_mask_part")
        x_probs, x_pv = sig("x_probs", TERMS * NG), sig("x_pv", TERMS * NG)
        path = Path()
        pool_ready = sem("pool_ready")
        ready = sem("ready")
        w_loaded, w_hi_done, w_split = sem("w_loaded"), sem("w_hi_done"), sem("w_split")
        c_loaded = sem("c_loaded")

        CHUNK = 2 * KT * D
        stage = probs[:].rearrange("p g h t n -> p (g h t n)")
        pieces = []
        for name, t, c in WNAMES:
            src = w[name].rearrange("(t p) c -> p t c", p=P)
            step = CHUNK // c
            for t0 in range(0, t, step):
                t1 = min(t, t0 + step)
                pieces.append((src[:, t0:t1, :], W[name][0][:, t0:t1, :], W[name][1][:, t0:t1, :]))
        STAGES = 4
        n_pieces = len(pieces)
        half = [stage[:, s * CHUNK:(s + 1) * CHUNK] for s in range(STAGES)]

        def staged(i, ap):
            t, c = ap.shape[1], ap.shape[2]
            return half[i % STAGES][:, 0:t * c].rearrange("p (t c) -> p t c", t=t)

        v_src = [w["wv"][r].rearrange("(t p) c -> p t c", p=P) for r in range(4)]
        bias_f = probs1[:].rearrange("p h t n -> p (h t n)")[0:1, 2 * KT * D:2 * KT * D + 4 * D]
        v_w = probs1[:].rearrange("p h t n -> p (h t n)")[:, 0:2 * KT * D].rearrange("p (r t c) -> p r t c", r=2, t=KT)
        N_CONST = 2 + 8 + 3 + 4
        block = ctx.enter_context(nc.Block())

        @block.sync
        def _(sp):
            sp.dma_start(v_w[:, 0], v_src[0]).then_inc(c_loaded, 16)
            sp.dma_start(v_w[:, 1], v_src[1]).then_inc(c_loaded, 16)
            for r, row in enumerate(("g1", "e1", "g2", "e2", "lg1", "lb1", "lg2", "lb2")):
                sp.dma_start(norm[:, r, :], w[row].partition_broadcast(P)).then_inc(c_loaded, 16)
            sp.dma_start(bq_c, w["bq"]).then_inc(c_loaded, 16)
            sp.dma_start(bk_c, w["bk"]).then_inc(c_loaded, 16)
            sp.dma_start(b1_c, w["b1"]).then_inc(c_loaded, 16)
            for k, row in enumerate((w["bv"][0], w["bv"][1], w["bo"], w["b2"])):
                sp.dma_start(bias_f[0:1, k * D:(k + 1) * D], row.rearrange("(a c) -> a c", a=1)).then_inc(c_loaded, 16)
            for i, (src, hi, lo) in enumerate(pieces):
                if i >= STAGES:
                    sp.wait_ge(w_split, i - STAGES + 1)
                sp.dma_start(staged(i, src), src).then_inc(w_loaded, 16)
                sp.wait_ge(w_loaded, 16 * (i + 1))

            def stack(graph, split, stacked, dst, free):
                sp.wait_ge(split.sem, split.at(graph))
                if later(graph):
                    sp.wait_ge(free.sem, free.before(graph))
                for h in range(GH):
                    for s in range(3):
                        for t in range(2):
                            part = qk_lo if (s, t) in ((2, 0), (1, 1)) else qk_hi
                            sp.dma_start(dst[s * DH:(s + 1) * DH, t, h:H:GH, :].bitcast(F32),
                                         part[h * DH:(h + 1) * DH, t, :, :].bitcast(F32)
                                         ).then_inc(stacked[h].sem, 16)

            def body(rest, attn, proj):
                if proj is not None:
                    if later(proj):
                        sp.wait_ge(xt_split.sem, xt_split.before(proj))
                    sp.dma_start(xt[:], xT[proj - path.general * G].rearrange("(t p) n -> p t n", p=P)).then_inc(ld_xt.sem, 16)
                if rest is not None:
                    if later(rest):
                        sp.wait_ge(off_done.sem, off_done.before(rest))
                    sp.dma_start(adj_q[:], adj[rest - path.general * G].rearrange("(t p) n -> p t n", p=P)).then_inc(ld_adj_r.sem, 16)
                    sp.dma_start(adj_k[:], adjT[rest - path.general * G].rearrange("(t p) n -> p t n", p=P)).then_inc(ld_adj_r.sem, 16)
                if attn is not None:
                    if path.general:
                        sp.wait_ge(result_done.sem, result_done.before(attn))
                    elif later(attn):
                        sp.wait_ge(known_done.sem, known_done.before(attn))
                    sp.dma_start(adj_a[:], adjT[attn - path.general * G].rearrange("(t p) n -> p t n", p=P)).then_inc(ld_adj_a.sem, 16)
                    if later(attn):
                        sp.wait_ge(res_a_done.sem, res_a_done.before(attn))
                    sp.dma_start(xn[:], x[attn - path.general * G].rearrange("(t p) c -> p t c", p=P)).then_inc(ld_xn.sem, 16)
                if attn is not None and path.general:
                    i = attn - G
                    for k in range(2):
                        if k:
                            sp.wait_ge(x_pv.sem, x_pv.at(i, NG))
                        for dst, src in ((act[:, 0], v_src[2 + k]), (act[:, 1], v_src[0]),
                                         (low_max[0:1, :], w["bv"][2 + k:3 + k, :]), (leaky[0:1, :], w["bv"][0:1, :])):
                            sp.dma_start(dst, src).then_inc(x_loaded.sem, 16)
                if rest is not None:
                    stack(rest, rqk_split, stacked_r, stack_r, str_mm)
                if proj is not None:
                    stack(proj, qk_split, stacked_a, stack_a, sta_mm)
                if rest is not None:
                    sp.wait_ge(result_done.sem, result_done.at(rest))
                    sp.dma_start(out[rest - path.general * G].rearrange("(t p) c -> p t c", p=P), result[:]).then_inc(stored.sem, 16)

            turns(sp, body)
            sp.wait_ge(stored.sem, stored.at(G - 1))
            sp.wait_ge(flag_ready, 1)
            found = sp.value_load(flag[0:1, 0:1], min_val=0, max_val=P)
            with sp.If(found > 0):
                path.general = True
                with sp.Fori(0, G) as i:
                    graph = i + G
                    body(None, None, graph)
                    body(None, graph, None)
                    body(graph, None, None)
                sp.wait_ge(stored.sem, stored.at(2 * G - 1))
                path.general = False

        @block.gpsimd
        def _(pool):
            nc.gpsimd.memset(ident[:], 0.0).then_inc(pool_ready, 1)
            nc.gpsimd.memset(ones[:], 1.0).then_inc(pool_ready, 1)
            nc.gpsimd.memset(power[:], -0.5).then_inc(pool_ready, 1)
            nc.gpsimd.memset(eps[:], EPS).then_inc(pool_ready, 1)
            nc.gpsimd.memset(carrier[:], 0.0).then_inc(pool_ready, 1)
            nc.gpsimd.memset(lowest[:], float(NT * N)).then_inc(pool_ready, 1)
            for tile in (bias_r, shift_a, shift_r):
                nc.gpsimd.memset(tile[:].bitcast(F32), 0.0).then_inc(pool_ready, 1)
            pool.wait_ge(pool_ready, 6)
            nc.gpsimd.affine_select(out=ident[:], in_=ident[:], compare_op=ALU.not_equal, fill=1.0,
                                    base=0, pattern=[[-1, P]], channel_multiplier=1).then_inc(pool_ready, 1)

            def make_rstd(k, graph):
                pool.wait_ge(ln_mv[k].sem, ln_mv[k].at(graph))
                nc.gpsimd.tensor_tensor(rstd[:, k, 0, :], mv[:, k, :, 1], eps[:], ALU.add).then_inc(ln_var[k].sem, 1)
                pool.wait_ge(ln_var[k].sem, ln_var[k].at(graph))
                nc.gpsimd.tensor_tensor(rstd[:, k, 1, :], rstd[:, k, 0, :], power[:], ALU.pow).then_inc(ln_rstd[k].sem, 1)

            def body(rest, attn, proj):
                if rest is not None:
                    for c in range(NCH):
                        pool.wait_ge(act_hi_done.sem, act_hi_done.at(rest, c + 1))
                        nc.gpsimd.tensor_tensor(act_lo[:, c % 2], act[:, c % 2], act_hi[:, c % 2], ALU.subtract
                                                ).then_inc(act_split.sem, 1)
                    make_rstd(LN_M, rest)
                if attn is not None:
                    pool.wait_ge(rel1_done.sem, rel1_done.at(attn))
                    if later(attn):
                        pool.wait_ge(pv1_mm.sem, pv1_mm.before(attn))
                    for p in range(PAIRS):
                        g, q = p // 2, p % 2
                        pool.wait_ge(probs_a.sem, probs_a.at(attn, p + 1))
                        if g:
                            pool.wait_ge(pv1_mm.sem, pv1_mm.at(attn, g))
                        for h in range(2 * q, 2 * q + 2):
                            last = nc.gpsimd.tensor_tensor(probs1[:, h], probs[:, g, h], rel1[:], ALU.mult)
                        last.then_inc(probs1_done.sem, 1)
                    if path.general:
                        i = attn - G
                        pool.wait_ge(pv1_mm.sem, pv1_mm.at(attn))
                        for k in range(TERMS):
                            pool.wait_ge(x_masked.sem, x_masked.at(i, k + 1))
                            for g in range(NG):
                                if k or g:
                                    pool.wait_ge(x_pv.sem, x_pv.at(i, k * NG + g))
                                for h in range(GH):
                                    last = nc.gpsimd.tensor_tensor(probs1[:, h], probs[:, g, h], rel1[:], ALU.mult)
                                last.then_inc(x_probs.sem, 1)
                    pool.wait_ge(att_hi_done.sem, att_hi_done.at(attn))
                    nc.gpsimd.tensor_tensor(att_lo[:], att[:], att_hi[:], ALU.subtract).then_inc(att_split.sem, 1)
                    make_rstd(LN_A, attn)
                if proj is not None:
                    pool.wait_ge(xt_hi_done.sem, xt_hi_done.at(proj))
                    nc.gpsimd.tensor_tensor(xt_lo[:], xt[:], xt_hi[:], ALU.subtract).then_inc(xt_split.sem, 1)
                if rest is not None:
                    make_rstd(LN_H, rest)
                    make_rstd(LN_O, rest)
                    pool.wait_ge(ln_done[LN_O].sem, ln_done[LN_O].at(rest))
                    if later(rest):
                        pool.wait_ge(stored.sem, stored.before(rest))
                    nc.gpsimd.tensor_tensor(result[:], y[:], x2[:], ALU.add).then_inc(result_done.sem, 1)

            turns(pool, body)
            pool.wait_ge(flag_ready, 1)
            found = pool.value_load(flag[0:1, 0:1], min_val=0, max_val=P)
            with pool.If(found > 0):
                path.general = True
                with pool.Fori(0, G) as i:
                    graph = i + G
                    pool.wait_ge(stored.sem, stored.before(graph))
                    body(None, None, graph)
                    pool.wait_ge(v_done.sem, v_done.at(graph))
                    for s in stacked_a:
                        pool.wait_ge(s.sem, s.at(graph))
                    body(None, graph, None)
                    pool.wait_ge(ln_done[LN_A].sem, ln_done[LN_A].at(graph))
                    body(graph, None, None)
                path.general = False

        @block.scalar
        def _(act_e):
            for i, (src, hi, lo) in enumerate(pieces):
                act_e.wait_ge(w_loaded, 16 * (i + 1))
                nc.scalar.activation(hi, staged(i, src), ACT.Copy).then_inc(w_hi_done, 1)

            def hi_part(dst, b, mm, graph, done):
                act_e.wait_ge(mm.sem, mm.at(graph))
                nc.scalar.activation(dst[:], bank[b][:], ACT.Copy).then_inc(done.sem, 1)

            def body(rest, attn, proj):
                if rest is not None:
                    hi_part(x1t_hi, B_X1T, x1t_mm, rest, x1t_hi_done)
                    for c in range(NCH):
                        act_e.wait_ge(up_mm.sem, up_mm.at(rest, c + 1))
                        if c >= 2:
                            act_e.wait_ge(act_split.sem, act_split.at(rest, c - 1))
                        for f in range(CH):
                            t = CH * c + f
                            last = nc.scalar.activation(act[:, c % 2, f], bank[B_UP[c]][:, f], ACT.Gelu,
                                                        bias=b1_c[:, t:t + 1])
                            last.then_inc(act_done.sem, 1) if f == CH - 1 else None
                if attn is not None:
                    if rest is not None:
                        if later(rest):
                            act_e.wait_ge(pvr_mm.sem, pvr_mm.before(rest))
                    for p in range(PAIRS):
                        g, q = p // 2, p % 2
                        act_e.wait_ge(sta_mm.sem, sta_mm.at(attn, p + 1))
                        nc.scalar.activation(probs[:, g, 2 * q:2 * q + 2], scores[p % 2][:], ACT.Exp, scale=SCALE
                                             ).then_inc(probs_a.sem, 1)
                if rest is not None:
                    hi_part(x2t_hi, B_X2T, x2t_mm, rest, x2t_hi_done)
                    if attn is not None:
                        for s in stacked_a:
                            act_e.wait_ge(s.sem, s.at(attn))
                    for t, b in ((0, B_RQ), (1, B_RK)):
                        act_e.wait_ge(rq_mm.sem, rq_mm.at(rest, t + 1))
                        nc.scalar.activation(qk_hi[:, t], bank[b][:], ACT.Copy).then_inc(rqk_hi_done.sem, 1)
                    act_e.wait_ge(rv_mm.sem, rv_mm.at(rest))
                    nc.scalar.activation(v_r[:], bank[B_RV][:], ACT.Copy).then_inc(rv_done.sem, 1)
                if rest is not None:
                    act_e.wait_ge(rmt_mm.sem, rmt_mm.at(rest))
                    nc.scalar.activation(low_max[:], bank[B_RMT][0:H, 0, :], ACT.Copy, scale=ALPHA
                                         ).then_inc(low_max_done.sem, 1)

                    def low(p):
                        g, q = p // 2, p % 2
                        act_e.wait_ge(str_mm.sem, str_mm.at(rest, p + 1))
                        if q == 0 and attn is not None:
                            act_e.wait_ge(pva_mm.sem, pva_mm.at(attn, g + 1))
                            act_e.wait_ge(probs1_done.sem, probs1_done.at(attn, 2 * g + 2))
                        nc.scalar.activation(probs[:, g, 2 * q:2 * q + 2], scores[p % 2][:], ACT.Copy, scale=ALPHA
                                             ).then_inc(low_done.sem, 1)

                    def exp(p):
                        g, q = p // 2, p % 2
                        act_e.wait_ge(sub_mm.sem, sub_mm.at(rest, p + 1))
                        nc.scalar.activation(probs[:, g, 2 * q:2 * q + 2], scores[p % 2][:], ACT.Exp
                                             ).then_inc(probs_r.sem, 1)

                    low(0)
                    for p in range(PAIRS):
                        if p + 1 < PAIRS:
                            low(p + 1)
                        exp(p)
                if proj is not None:
                    for t, (b, col) in enumerate(((B_Q, bq_c), (B_K, bk_c))):
                        act_e.wait_ge(q_mm.sem, q_mm.at(proj, t + 1))
                        if t == 0 and rest is not None:
                            for s in stacked_r:
                                act_e.wait_ge(s.sem, s.at(rest))
                        for m in range(NG):
                            last = nc.scalar.activation(qk_hi[:, t, m], bank[b][:, m], ACT.Identity, bias=col[:, m:m + 1])
                        last.then_inc(qk_hi_done.sem, 1)
                    if attn is not None:
                        act_e.wait_ge(pv1_mm.sem, pv1_mm.at(attn))
                    for t in range(NT):
                        act_e.wait_ge(v_mm.sem, v_mm.at(proj, t + 1))
                        nc.scalar.activation(v_a[:, t], bank[B_V[t]][:], ACT.Copy
                                             ).then_inc(v_done.sem, 1)
                if rest is not None:
                    hi_part(n1t_hi, B_N1T, n1t_mm, rest, n1t_hi_done)

            turns(act_e, body)
            act_e.wait_ge(flag_ready, 1)
            found = act_e.value_load(flag[0:1, 0:1], min_val=0, max_val=P)
            with act_e.If(found > 0):
                path.general = True
                with act_e.Fori(0, G) as i:
                    graph = i + G
                    act_e.wait_ge(stored.sem, stored.before(graph))
                    body(None, None, graph)
                    act_e.wait_ge(v_done.sem, v_done.at(graph))
                    for s in stacked_a:
                        act_e.wait_ge(s.sem, s.at(graph))
                    body(None, graph, None)
                    act_e.wait_ge(ln_done[LN_A].sem, ln_done[LN_A].at(graph))
                    body(graph, None, None)
                path.general = False

        @block.vector
        def _(dve):
            dve.wait_ge(pool_ready, 10)
            nc.vector.tensor_copy(identb[:], ident[:]).then_inc(ready, 1)
            nc.vector.tensor_copy(onesr[:], ones[0:SHIFT, :]).then_inc(ready, 1)
            for r in range(2):
                nc.vector.tensor_copy(selr[32 * r:32 * r + 32, :], ident[0:32, 0:H]).then_inc(ready, 1)
            dve.wait_ge(c_loaded, 16 * N_CONST)
            nc.vector.tensor_tensor(bias_f[:, D:2 * D], bias_f[:, D:2 * D], bias_f[:, 0:D], ALU.subtract).then_inc(ready, 1)
            nc.vector.tensor_tensor(v_w[:, 1], v_w[:, 1], v_w[:, 0], ALU.subtract).then_inc(ready, 1)
            dve.wait_ge(ready, 6)
            nc.vector.tensor_copy(bias_r[0:1, :], bias_f).then_inc(ready, 1)
            for r in range(2):
                nc.vector.tensor_copy(W["wv"][0][:, :, r * D:(r + 1) * D], v_w[:, r]).then_inc(ready, 1)
            dve.wait_ge(ready, 9)
            nc.vector.tensor_tensor(bias_r[32:33, :], bias_f, bias_r[0:1, :], ALU.subtract).then_inc(ready, 1)
            for r in range(2):
                nc.vector.tensor_tensor(W["wv"][1][:, :, r * D:(r + 1) * D], v_w[:, r],
                                        W["wv"][0][:, :, r * D:(r + 1) * D], ALU.subtract).then_inc(ready, 1)
            for i, (src, hi, lo) in enumerate(pieces):
                dve.wait_ge(w_hi_done, i + 1)
                nc.vector.tensor_tensor(lo, staged(i, src), hi, ALU.subtract).then_inc(w_split, 1)

            def flat(ap):
                return ap[:].rearrange("p a n -> p (a n)")

            def lo_part(dst, hi, b, hi_done, graph, done):
                dve.wait_ge(hi_done.sem, hi_done.at(graph))
                nc.vector.tensor_tensor(flat(dst), flat(bank[b]), flat(hi), ALU.subtract
                                        ).then_inc(done.sem, 1)

            def maxima(mm, dst, graph, done):
                for p in range(PAIRS):
                    dve.wait_ge(mm.sem, mm.at(graph, p + 1))
                    nc.vector.tensor_reduce(dst[:, :, p:H:GH].rearrange("p t h -> p h t"), scores[p % 2][:],
                                            AX.X, ALU.max).then_inc(done.sem, 1)

            def shift(src, dst, graph, hi_done, done):
                i = nc.vector.tensor_scalar(dst[0:H, :], src, -1.0, None, ALU.mult)
                i.then_inc(hi_done.sem, 1)
                dve.wait_ge(hi_done.sem, hi_done.at(graph))
                return nc.vector.scalar_tensor_tensor(dst[32:32 + H, :], src, -1.0, dst[0:H, :], ALU.mult,
                                                      ALU.subtract).then_inc(done.sem, 1)

            def heads_out(pv, graph, b_o, b_den, rden_done, done):
                dve.wait_ge(pv.sem, pv.at(graph))
                nc.vector.reciprocal(att[:], bank[b_den][:]).then_inc(rden_done.sem, 1)
                dve.wait_ge(rden_done.sem, rden_done.at(graph))
                nc.vector.tensor_tensor(att[:], bank[b_o][:], att[:], ALU.mult
                                        ).then_inc(done.sem, 1)

            def statistics(k, src, graph):
                for t in range(NT):
                    nc.vector.bn_stats(stats[:, k, t], src[:, t]).then_inc(ln_stats[k].sem, 1)
                dve.wait_ge(ln_stats[k].sem, ln_stats[k].at(graph))
                nc.vector.tensor_copy(carrier[:, 0:1], carrier[:, 1:2])
                for t in range(NT):
                    nc.vector.bn_aggr(mv[:, k, t], stats[:, k, t]).then_inc(ln_mv[k].sem, 1)

            def normalise(k, src, gain, offset, dst, graph):
                dve.wait_ge(ln_mv[k].sem, ln_mv[k].at(graph))
                for t in range(NT):
                    nc.vector.scalar_tensor_tensor(dst[:, t], src[:, t], mv[:, k, t, 0:1], norm[:, gain], ALU.subtract,
                                                          ALU.mult).then_inc(ln_mid[k].sem, 1)
                dve.wait_ge(ln_rstd[k].sem, ln_rstd[k].at(graph))
                dve.wait_ge(ln_mid[k].sem, ln_mid[k].at(graph))
                for t in range(NT):
                    nc.vector.scalar_tensor_tensor(dst[:, t], dst[:, t], rstd[:, k, 1, t:t + 1], norm[:, offset],
                                                   ALU.mult, ALU.add).then_inc(ln_done[k].sem, 1)

            def further_terms(attn):
                i = attn - G
                dve.wait_ge(probs1_done.sem, probs1_done.at(attn))
                for k in range(TERMS):
                    if k:
                        dve.wait_ge(x_pv.sem, x_pv.at(i, k * NG))
                    if k < 2:
                        dve.wait_ge(x_loaded.sem, x_loaded.at(i, 64 * (k + 1)))
                        row = low_max[0:1, :]
                        nc.vector.tensor_tensor(act[:, 0], act[:, 0], act[:, 1], ALU.subtract).then_inc(x_diff.sem, 1)
                        nc.vector.tensor_tensor(row, row, leaky[0:1, :], ALU.subtract).then_inc(x_diff.sem, 1)
                        dve.wait_ge(x_diff.sem, x_diff.at(i, 2 * k + 2))
                        nc.vector.tensor_copy(act_hi[:, 0], act[:, 0]).then_inc(x_high.sem, 1)
                        nc.vector.tensor_copy(shift_r[0:1, :], row).then_inc(x_high.sem, 1)
                        dve.wait_ge(x_high.sem, x_high.at(i, 2 * k + 2))
                        nc.vector.tensor_tensor(act_lo[:, 0], act[:, 0], act_hi[:, 0], ALU.subtract).then_inc(x_ready.sem, 1)
                        nc.vector.tensor_tensor(shift_r[32:33, :], row, shift_r[0:1, :], ALU.subtract).then_inc(x_ready.sem, 1)
                        dve.wait_ge(x_v.sem, x_v.at(i, k + 1))
                        nc.vector.tensor_copy(v_r[:], bank[B_WO][:]).then_inc(x_vr.sem, 1)
                        nc.vector.tensor_scalar(rel1[:], adj_a[:], 2 + k, None, ALU.is_equal).then_inc(x_masked.sem, 1)
                    else:
                        nc.vector.tensor_scalar(v_r[:], v_a[:, :, 0], -1.0, None, ALU.mult).then_inc(x_vr.sem, 1)
                        nc.vector.tensor_scalar(rel1[:], adj_a[:], 0, None, ALU.is_lt).then_inc(x_mask_part.sem, 1)
                        dve.wait_ge(x_mask_part.sem, x_mask_part.at(i))
                        nc.vector.scalar_tensor_tensor(rel1[:], adj_a[:], 3, rel1[:], ALU.is_gt, ALU.add
                                                       ).then_inc(x_masked.sem, 1)
                dve.wait_ge(x_pv.sem, x_pv.at(i))

            def body(rest, attn, proj):
                if rest is not None:
                    dve.wait_ge(ld_adj_r.sem, ld_adj_r.at(rest))
                    for src, dst in ((adj_q, off_q), (adj_k, off_k)):
                        nc.vector.tensor_scalar(dst[:], src[:], 0, NEG, ALU.is_le, ALU.mult).then_inc(off_done.sem, 1)
                if attn is not None:
                    dve.wait_ge(ld_adj_a.sem, ld_adj_a.at(attn))
                    if later(attn):
                        dve.wait_ge(probs1_done.sem, probs1_done.before(attn))
                    nc.vector.tensor_scalar(rel1[:], adj_a[:], 1, None, ALU.is_equal).then_inc(rel1_done.sem, 1)
                    if not path.general:
                        dve.wait_ge(rel1_done.sem, rel1_done.at(attn))
                        nc.vector.scalar_tensor_tensor(adj_a[:], adj_a[:], 0, rel1[:], ALU.is_equal, ALU.add,
                                                       accum_out=known[:]).then_inc(known_done.sem, 1)
                if rest is not None:
                    lo_part(x1t_lo, x1t_hi, B_X1T, x1t_hi_done, rest, x1t_split)
                    for c in range(NCH):
                        dve.wait_ge(act_done.sem, act_done.at(rest, c + 1))
                        if c >= 2:
                            dve.wait_ge(down_part.sem, down_part.at(rest, c - 1))
                        nc.vector.tensor_copy(act_hi[:, c % 2], act[:, c % 2]).then_inc(act_hi_done.sem, 1)
                if attn is not None:
                    maxima(sa_mm, mx_a, attn, mx_a_done)
                    if not path.general:
                        dve.wait_ge(known_done.sem, known_done.at(attn))
                        nc.vector.tensor_tensor(lowest[:], lowest[:], known[:], ALU.min).then_inc(lowest_done.sem, 1)
                if rest is not None:
                    dve.wait_ge(down_mm.sem, down_mm.at(rest))
                    if later(rest):
                        dve.wait_ge(stored.sem, stored.before(rest))
                    nc.vector.tensor_tensor(res[:], bank[B_DOWN][:], x1[:], ALU.add
                                            ).then_inc(res_m_done.sem, 1)
                    dve.wait_ge(res_m_done.sem, res_m_done.at(rest))
                    statistics(LN_M, res, rest)
                if attn is not None:
                    dve.wait_ge(amt_mm.sem, amt_mm.at(attn))
                    shift(bank[B_AMT][0:H, 0, :], shift_a, attn, ashift_hi, ashift)
                if rest is not None:
                    normalise(LN_M, res, G2, E2, x2, rest)
                    lo_part(x2t_lo, x2t_hi, B_X2T, x2t_hi_done, rest, x2t_split)
                    for t, b in ((0, B_RQ), (1, B_RK)):
                        dve.wait_ge(rqk_hi_done.sem, rqk_hi_done.at(rest, t + 1))
                        nc.vector.tensor_tensor(qk_lo[:, t], bank[b][:], qk_hi[:, t], ALU.subtract
                                                ).then_inc(rqk_split.sem, 1)
                if rest is not None:
                    maxima(sr_mm, mx_r, rest, mx_r_done)
                if attn is not None:
                    if later(rest):
                        dve.wait_ge(hn_mm.sem, hn_mm.before(rest))
                    if path.general:
                        further_terms(attn)
                    heads_out(pv1_mm, attn, B_AO, B_ADEN, rden_a, att_a)
                    dve.wait_ge(att_a.sem, att_a.at(attn))
                    nc.vector.tensor_copy(att_hi[:], att[:]).then_inc(att_hi_done.sem, 1)
                if rest is not None:
                    dve.wait_ge(low_max_done.sem, low_max_done.at(rest))
                    nc.vector.tensor_tensor(leaky[:], bank[B_RMT][0:H, 0, :], low_max[:], ALU.max).then_inc(leaky_done.sem, 1)
                    dve.wait_ge(leaky_done.sem, leaky_done.at(rest))
                    shift(leaky[:], shift_r, rest, rshift_hi, rshift)
                    for p in range(PAIRS):
                        dve.wait_ge(low_done.sem, low_done.at(rest, p + 1))
                        g, q = p // 2, p % 2
                        nc.vector.tensor_tensor(scores[p % 2][:], scores[p % 2][:], probs[:, g, 2 * q:2 * q + 2], ALU.max
                                                ).then_inc(leaky_scores.sem, 1)
                if attn is not None:
                    dve.wait_ge(wo_mm.sem, wo_mm.at(attn))
                    dve.wait_ge(ld_xn.sem, ld_xn.at(attn))
                    nc.vector.tensor_tensor(res[:], bank[B_WO][:], xn[:], ALU.add
                                            ).then_inc(res_a_done.sem, 1)
                    dve.wait_ge(res_a_done.sem, res_a_done.at(attn))
                    statistics(LN_A, res, attn)
                    normalise(LN_A, res, G1, E1, x1, attn)
                if proj is not None:
                    dve.wait_ge(ld_xt.sem, ld_xt.at(proj))
                    if later(proj):
                        dve.wait_ge(v_mm.sem, v_mm.before(proj))
                    nc.vector.tensor_copy(xt_hi[:], xt[:]).then_inc(xt_hi_done.sem, 1)
                if rest is not None:
                    if attn is not None:
                        dve.wait_ge(att_split.sem, att_split.at(attn))
                    heads_out(pvr_mm, rest, B_RO, B_RDEN, rden_r, att_r_done)
                if proj is not None:
                    for t, (b, col) in enumerate(((B_Q, bq_c), (B_K, bk_c))):
                        dve.wait_ge(qk_hi_done.sem, qk_hi_done.at(proj, t + 1))
                        for m in range(NG):
                            last = nc.vector.scalar_tensor_tensor(qk_lo[:, t, m], bank[b][:, m], col[:, m:m + 1],
                                                                  qk_hi[:, t, m], ALU.add, ALU.subtract)
                        last.then_inc(qk_split.sem, 1)
                if rest is not None:
                    dve.wait_ge(hn_mm.sem, hn_mm.at(rest))
                    statistics(LN_H, bank[B_HN], rest)
                    normalise(LN_H, bank[B_HN], LG1, LB1, n1, rest)
                    lo_part(n1t_lo, n1t_hi, B_N1T, n1t_hi_done, rest, n1t_split)
                    dve.wait_ge(ffn_mm.sem, ffn_mm.at(rest))
                    statistics(LN_O, bank[B_FFN], rest)
                    normalise(LN_O, bank[B_FFN], LG2, LB2, y, rest)

            turns(dve, body)
            dve.wait_ge(lowest_done.sem, lowest_done.at(G - 1))
            nc.vector.tensor_scalar(bad[:], lowest[:], float(NT * N), None, ALU.is_lt).then_inc(bad_done, 1)
            dve.wait_ge(bad_mm, 1)
            nc.vector.tensor_copy(flag[:], bank[B_X1T][0:1, 0, 0:1]).then_inc(flag_ready, 1)
            dve.wait_ge(flag_ready, 1)
            found = dve.value_load(flag[0:1, 0:1], min_val=0, max_val=P)
            with dve.If(found > 0):
                path.general = True
                with dve.Fori(0, G) as i:
                    graph = i + G
                    dve.wait_ge(stored.sem, stored.before(graph))
                    body(None, None, graph)
                    dve.wait_ge(v_done.sem, v_done.at(graph))
                    for s in stacked_a:
                        dve.wait_ge(s.sem, s.at(graph))
                    body(None, graph, None)
                    dve.wait_ge(ln_done[LN_A].sem, ln_done[LN_A].at(graph))
                    body(graph, None, None)
                path.general = False

        @block.tensor
        def _(pe):
            mm = nc.tensor.matmul

            def products(dst, lhs, rhs, depth, start=True, stop=True, skip=False):
                steps = [(i, j, t) for i, j in ((0, 0), (0, 1), (1, 0)) for t in range(depth)]
                for n, (i, j, t) in enumerate(steps):
                    last = mm(dst, lhs(i, t), rhs(j, t), start=start and n == 0, stop=stop and n == len(steps) - 1,
                              skip_group_check=skip)
                return last

            def add_bias(dst, row, skip=False):
                return mm(dst, onesr[:], row, start=False, stop=True, skip_group_check=skip)

            def cols(pair, m):
                return lambda i, t: pair[i][:, t, m * P:(m + 1) * P]

            def whole(pair):
                return lambda j, t: pair[j][:, t, :]

            def transposed(dst, src, done):
                for k in range(KT):
                    for t in range(NT):
                        last = nc.tensor.transpose(dst[:, k, t * P:(t + 1) * P], src[:, t, k * P:(k + 1) * P], ident[:])
                last.then_inc(done.sem, 1)

            def projection(name, xts, b):
                for m in range(NG):
                    last = products(bank[b][:, m], cols(W[name], m), whole(xts), KT)
                return last

            def score_rows(stack, graph, stacked, done, read, mask=None):
                for p in range(PAIRS):
                    pe.wait_ge(stacked[p].sem, stacked[p].at(graph))
                    if p >= 2:
                        pe.wait_ge(read.sem, read.at(graph, p - 1))
                    for k, h in enumerate((p, p + GH)):
                        for t in range(NT):
                            dst = scores[p % 2][:, k, t]
                            last = mm(dst, stack[:, 0, h, t * P:(t + 1) * P], stack[:, 1, h, :], start=True,
                                      stop=mask is None)
                            if mask is not None:
                                last = mm(dst, identb[:], mask[:, t, :], start=False, stop=True)
                    last.then_inc(done.sem, 1)

            def maxima_rows(src, b, graph, ready_max, done):
                pe.wait_ge(ready_max.sem, ready_max.at(graph))
                for t in range(NT):
                    last = nc.tensor.transpose(bank[b][0:H, 0, t * P:(t + 1) * P], src[:, t, :], ident[:])
                last.then_inc(done.sem, 1)

            def score_cols(stack, p, graph, read, mask=None):
                if p >= 2:
                    pe.wait_ge(read.sem, read.at(graph, p - 1))
                for k in range(2):
                    h = 2 * p + k
                    for t in range(NT):
                        dst = scores[p % 2][:, k, t]
                        last = mm(dst, stack[:, 1, h, t * P:(t + 1) * P], stack[:, 0, h, :], start=t == 0, stop=False,
                                  skip_group_check=True)
                        if mask is not None:
                            last = mm(dst, identb[:], mask[:, t, :], start=False, stop=False, skip_group_check=True)
                return last

            def subtract_maxima(shifts, p):
                for k in range(2):
                    h = 2 * p + k
                    for t in range(NT):
                        last = mm(scores[p % 2][:, k, t], selr[:, h:h + 1].broadcast_to([SHIFT, P]), shifts[:],
                                  start=False, stop=True, skip_group_check=True)
                return last

            def values(b, g, v, pr, first, stop):
                for t in range(NT):
                    for h in range(GH):
                        last = mm(bank[b][h * DH:(h + 1) * DH, g, :], v(t, g * GH + h), pr(h, t),
                                  start=first and t == 0, stop=stop and t == NT - 1, skip_group_check=True)
                return last

            def plain(g):
                return lambda h, t: probs[:, g, h, t]

            def rows_sum(b, g):
                return values(b, g, lambda t, h: ones[:, 0:DH], plain(g), g == 0, True)

            pe.wait_ge(ready, 12)
            pe.wait_ge(w_split, n_pieces)

            def body(rest, attn, proj):
                if rest is not None:
                    pe.wait_ge(ln_done[LN_A].sem, ln_done[LN_A].at(rest))
                    if attn is not None:
                        pe.wait_ge(v_done.sem, v_done.at(attn))
                        pe.wait_ge(qk_split.sem, qk_split.at(attn))
                    transposed(bank[B_X1T], x1, x1t_mm)
                    pe.wait_ge(x1t_split.sem, x1t_split.at(rest))

                    def up(c):
                        if c == 1 and later(rest):
                            pe.wait_ge(ln_mid[LN_O].sem, ln_mid[LN_O].before(rest))
                        elif c >= 2:
                            pe.wait_ge(act_done.sem, act_done.at(rest, c - 1))
                        for f in range(CH):
                            last = products(bank[B_UP[c]][:, f], cols(W["w1"], c * CH + f), whole((x1t_hi, x1t_lo)), KT)
                        last.then_inc(up_mm.sem, 1)

                    def down(c):
                        pe.wait_ge(act_split.sem, act_split.at(rest, c + 1))
                        parts = (act_hi, act_lo)
                        for t in range(NT):
                            last = products(bank[B_DOWN][:, t],
                                            lambda i, f: parts[i][:, c % 2, f, t * P:(t + 1) * P],
                                            lambda j, f: W["w2"][j][:, c * CH + f, :], CH,
                                            start=c == 0 and t == 0, stop=False, skip=True)
                        last.then_inc(down_part.sem, 1)
                        if c == NCH - 1:
                            for t in range(NT):
                                last = add_bias(bank[B_DOWN][:, t], b2_r, skip=True)
                            last.then_inc(down_mm.sem, 1)

                    up(0)
                    up(1)
                    down(0)
                    up(2)
                    down(1)
                    up(3)
                    down(2)
                if attn is not None:
                    score_rows(stack_a, attn, stacked_a, sa_mm, mx_a_done)
                if rest is not None:
                    down(3)
                if attn is not None:
                    pe.wait_ge(v_done.sem, v_done.at(attn))
                    maxima_rows(mx_a, B_AMT, attn, mx_a_done, amt_mm)
                    pe.wait_ge(ashift.sem, ashift.at(attn))
                    for p in range(PAIRS):
                        score_cols(stack_a, p, attn, probs_a)
                        subtract_maxima(shift_a, p).then_inc(sta_mm.sem, 1)
                if rest is not None:
                    pe.wait_ge(ln_done[LN_M].sem, ln_done[LN_M].at(rest))
                    transposed(bank[B_X2T], x2, x2t_mm)
                    pe.wait_ge(x2t_split.sem, x2t_split.at(rest))
                    for name, b in (("lq", B_RQ), ("lk", B_RK)):
                        projection(name, (x2t_hi, x2t_lo), b).then_inc(rq_mm.sem, 1)
                    parts = (x2t_hi, x2t_lo)
                    for t in range(NT):
                        last = products(bank[B_RV][:, t], lambda i, k: parts[i][:, k, t * P:(t + 1) * P],
                                        whole(W["lv"]), KT)
                    last.then_inc(rv_mm.sem, 1)
                if attn is not None:
                    pe.wait_ge(v_done.sem, v_done.at(attn))
                    if rest is not None:
                        pe.wait_ge(rqk_split.sem, rqk_split.at(rest))
                        pe.wait_ge(res_m_done.sem, res_m_done.at(rest))
                    for g in range(NG):
                        pe.wait_ge(probs_a.sem, probs_a.at(attn, 2 * g + 2))
                        values(B_AO, g, lambda t, h: v_a[:, t, 0, h * DH:(h + 1) * DH], plain(g), g == 0, False)
                        rows_sum(B_ADEN, g).then_inc(pva_mm.sem, 1)
                    for g in range(NG):
                        pe.wait_ge(probs1_done.sem, probs1_done.at(attn, 2 * g + 2))
                        values(B_AO, g, lambda t, h: v_a[:, t, 1, h * DH:(h + 1) * DH], lambda h, t: probs1[:, h, t],
                               False, True).then_inc(pv1_mm.sem, 1)
                    if path.general:
                        i = attn - G
                        parts = (xt_hi, xt_lo)
                        wx = (act_hi, act_lo)
                        for k in range(TERMS):
                            if k < 2:
                                pe.wait_ge(x_ready.sem, x_ready.at(i, 2 * k + 2))
                                for t in range(NT):
                                    products(bank[B_WO][:, t], lambda a, c: parts[a][:, c, t * P:(t + 1) * P],
                                             lambda a, c: wx[a][:, 0, c, :], KT, stop=False)
                                    last = mm(bank[B_WO][:, t], selr[:, 0:1].broadcast_to([SHIFT, P]), shift_r[:],
                                              start=False, stop=True)
                                last.then_inc(x_v.sem, 1)
                            pe.wait_ge(x_vr.sem, x_vr.at(i, k + 1))
                            for g in range(NG):
                                pe.wait_ge(x_probs.sem, x_probs.at(i, k * NG + g + 1))
                                values(B_AO, g, lambda t, h: v_r[:, t, h * DH:(h + 1) * DH], lambda h, t: probs1[:, h, t],
                                       False, True).then_inc(x_pv.sem, 1)
                if rest is not None:
                    pe.wait_ge(off_done.sem, off_done.at(rest))
                    score_rows(stack_r, rest, stacked_r, sr_mm, mx_r_done, off_q)
                    maxima_rows(mx_r, B_RMT, rest, mx_r_done, rmt_mm)
                    for p in range(2):
                        score_cols(stack_r, p, rest, probs_r, off_k).then_inc(str_mm.sem, 1)
                if attn is not None:
                    pe.wait_ge(att_split.sem, att_split.at(attn))
                    if rest is not None:
                        pe.wait_ge(rv_done.sem, rv_done.at(rest))
                    parts_a = (att_hi, att_lo)
                    for t in range(NT):
                        products(bank[B_WO][:, t], lambda i, g: parts_a[i][:, g, t * P:(t + 1) * P],
                                 whole(W["wo"]), NG, stop=False)
                        last = add_bias(bank[B_WO][:, t], bo_r)
                    last.then_inc(wo_mm.sem, 1)
                if rest is not None:
                    pe.wait_ge(rshift.sem, rshift.at(rest))
                    for p in range(PAIRS):
                        pe.wait_ge(leaky_scores.sem, leaky_scores.at(rest, p + 1))
                        subtract_maxima(shift_r, p).then_inc(sub_mm.sem, 1)
                        if p + 2 < PAIRS:
                            score_cols(stack_r, p + 2, rest, probs_r, off_k).then_inc(str_mm.sem, 1)
                    pe.wait_ge(rv_done.sem, rv_done.at(rest))
                    if attn is not None:
                        pe.wait_ge(att_a.sem, att_a.at(attn))
                    for g in range(NG):
                        pe.wait_ge(probs_r.sem, probs_r.at(rest, 2 * g + 2))
                        values(B_RO, g, lambda t, h: v_r[:, t, h * DH:(h + 1) * DH], plain(g), g == 0, True)
                        rows_sum(B_RDEN, g).then_inc(pvr_mm.sem, 1)
                if proj is not None:
                    pe.wait_ge(xt_split.sem, xt_split.at(proj))
                    projection("wq", (xt_hi, xt_lo), B_Q).then_inc(q_mm.sem, 1)
                    if rest is not None:
                        pe.wait_ge(att_r_done.sem, att_r_done.at(rest))
                    projection("wk", (xt_hi, xt_lo), B_K).then_inc(q_mm.sem, 1)
                if rest is not None:
                    pe.wait_ge(att_r_done.sem, att_r_done.at(rest))
                    if attn is not None:
                        pe.wait_ge(res_a_done.sem, res_a_done.at(attn))
                    transposed(bank[B_HN], att, hn_mm)
                if proj is not None:
                    parts_x = (xt_hi, xt_lo)
                    for t in range(NT):
                        if t == 1:
                            pe.wait_ge(qk_split.sem, qk_split.at(proj, 1))
                        dst = bank[B_V[t]][:].rearrange("p a n -> p (a n)")
                        products(dst, lambda i, k: parts_x[i][:, k, t * P:(t + 1) * P], whole(W["wv"]), KT, stop=False)
                        add_bias(dst, bv_r).then_inc(v_mm.sem, 1)
                if rest is not None:
                    pe.wait_ge(ln_done[LN_H].sem, ln_done[LN_H].at(rest))
                    if proj is not None:
                        pe.wait_ge(qk_split.sem, qk_split.at(proj))
                    transposed(bank[B_N1T], n1, n1t_mm)
                    pe.wait_ge(n1t_split.sem, n1t_split.at(rest))
                    parts_n, parts_2 = (n1t_hi, n1t_lo), (x2t_hi, x2t_lo)
                    for t in range(NT):
                        products(bank[B_FFN][:, t], lambda i, k: parts_2[i][:, k, t * P:(t + 1) * P],
                                 lambda j, k: W["wf"][j][:, KT + k, :], KT, stop=False)
                        last = products(bank[B_FFN][:, t], lambda i, k: parts_n[i][:, k, t * P:(t + 1) * P],
                                        lambda j, k: W["wf"][j][:, k, :], KT, start=False)
                    last.then_inc(ffn_mm.sem, 1)

            turns(pe, body)
            pe.wait_ge(bad_done, 1)
            mm(bank[B_X1T][0:1, 0, 0:1], bad[:], ones[:, 0:1], start=True, stop=True).then_inc(bad_mm, 1)
            pe.wait_ge(flag_ready, 1)
            found = pe.value_load(flag[0:1, 0:1], min_val=0, max_val=P)
            with pe.If(found > 0):
                path.general = True
                with pe.Fori(0, G) as i:
                    graph = i + G
                    pe.wait_ge(stored.sem, stored.before(graph))
                    body(None, None, graph)
                    pe.wait_ge(v_done.sem, v_done.at(graph))
                    for s in stacked_a:
                        pe.wait_ge(s.sem, s.at(graph))
                    body(None, graph, None)
                    pe.wait_ge(ln_done[LN_A].sem, ln_done[LN_A].at(graph))
                    body(graph, None, None)
                path.general = False

    return nc


_BIASES = {"bq": "L0_gnn_bq", "bk": "L0_gnn_bk", "bv": "L0_gnn_bv", "bo": "L0_gnn_bo", "b1": "L0_gnn_b1", "b2": "L0_gnn_b2",
           "g1": "L0_gnn_g1", "e1": "L0_gnn_beta1", "g2": "L0_gnn_g2", "e2": "L0_gnn_beta2",
           "lg1": "L1_gnn_g1", "lb1": "L1_gnn_b1", "lg2": "L1_gnn_g2", "lb2": "L1_gnn_b2"}
_WEIGHTS = {"wq": "L0_gnn_Wq", "wk": "L0_gnn_Wk", "wv": "L0_gnn_Wv", "wo": "L0_gnn_Wo", "w1": "L0_gnn_W1", "w2": "L0_gnn_W2",
            "lq": "L1_gnn_Wq", "lk": "L1_gnn_Wk", "lv": "L1_gnn_Wv"}


def kernel(**inputs):
    import numpy as np
    import concourse.bacc as bacc
    from concourse.bass_utils import run_bass_kernel_spmd

    nc = bacc.Bacc("TRN2", target_bir_lowering=False, num_devices=1)
    x, adj = np.asarray(inputs["x"]), np.asarray(inputs["adj"])
    data = {"x": x, "xT": x.transpose(0, 2, 1), "adj": adj, "adjT": adj.transpose(0, 2, 1),
            "wf": np.asarray(inputs["L1_gnn_Wffn"]).T}
    data |= {k: np.asarray(inputs[v]) for k, v in (_BIASES | _WEIGHTS).items()}
    for k in ("bq", "bk", "b1"):
        data[k] = data[k].reshape(-1, P).T
    data = {k: np.ascontiguousarray(v) for k, v in data.items()}
    ap = {k: nc.dram_tensor("in_" + k, v.shape, mybir.dt.from_np(v.dtype), kind="ExternalInput").ap()
          for k, v in data.items()}
    ap["out"] = nc.dram_tensor("out_0", (G, N, D), F32, kind="ExternalOutput").ap()
    build(nc, ap["x"], ap["xT"], ap["adj"], ap["adjT"], ap)
    r = run_bass_kernel_spmd(nc, [{"in_" + k: v for k, v in data.items()}], core_ids=[0])
    return r.results[0]["out_0"]
```
